# Optimizing a Trainium2 kernel written in Bass

```python
import numpy as np
import jax
import jax.numpy as jnp

def _softmax(x, axis=-1):
    return jax.nn.softmax(x, axis=axis)

def _gelu(x):
    return jax.nn.gelu(x, approximate=True)

def _silu(x):
    return jax.nn.silu(x)

def _sigmoid(x):
    return jax.nn.sigmoid(x)

def _layernorm(x, axis=-1, eps=1e-05):
    m = jnp.mean(x, axis=axis, keepdims=True)
    v = jnp.var(x, axis=axis, keepdims=True)
    return (x - m) / jnp.sqrt(v + eps)

def _scatter_add(tgt, idx, src, axis=0):
    return tgt.at[idx].add(src)

def _segment_sum(src, seg, n):
    return jax.ops.segment_sum(src, seg, n)
kernel_name = 'mk_seq_postln_d1_jaxref_r4_2034ee'

def setup_inputs(seed: int=0):
    np.random.seed(seed)
    _w = jnp.asarray

    def _L0_attn_setup():
        import jax, jax.numpy as jnp
        import numpy as np
        import math
        N_HEAD = 16
        N_EMBD = 256
        HEAD_D = N_EMBD // N_HEAD
        BASE = 2500

        def rope(Y):
            d = Y.shape[-1]
            t = Y.shape[-2]
            theta = BASE ** (-2.0 * jnp.arange(d // 2, dtype=Y.dtype) / d)
            theta2 = jnp.concatenate([theta, theta], axis=0)
            pos = jnp.arange(1, t + 1, dtype=Y.dtype)
            C = pos[:, None] * theta2[None, :]
            cos, sin = (jnp.cos(C), jnp.sin(C))
            Y2 = jnp.concatenate([-Y[..., d // 2:], Y[..., :d // 2]], axis=-1)
            return Y * cos + Y2 * sin
        key = jax.random.key(seed)
        ks = jax.random.split(key, 9)
        s = 0.02
        x = jax.random.normal(ks[0], (4, 512, N_EMBD), dtype=jnp.float32)
        Wq = jax.random.normal(ks[1], (N_EMBD, N_EMBD), dtype=jnp.float32) * s
        bq = jnp.zeros((N_EMBD,), dtype=jnp.float32)
        Wk = jax.random.normal(ks[2], (N_EMBD, N_EMBD), dtype=jnp.float32) * s
        bk = jnp.zeros((N_EMBD,), dtype=jnp.float32)
        Wv = jax.random.normal(ks[3], (N_EMBD, N_EMBD), dtype=jnp.float32) * s
        bv = jnp.zeros((N_EMBD,), dtype=jnp.float32)
        Wo = jax.random.normal(ks[4], (N_EMBD, N_EMBD), dtype=jnp.float32) * s
        bo = jnp.zeros((N_EMBD,), dtype=jnp.float32)
        return {'x': x, 'Wq': Wq, 'bq': bq, 'Wk': Wk, 'bk': bk, 'Wv': Wv, 'bv': bv, 'Wo': Wo, 'bo': bo}
    _L0_attn_in = _L0_attn_setup()

    def _L0_ffn_setup():
        import jax, jax.numpy as jnp
        import numpy as np
        D_IN, D_HID = (256, 1024)

        def _ternary(key, shape):
            return jax.random.randint(key, shape, -1, 2).astype(jnp.float32)

        def _tlin(x, w, s):
            return jnp.einsum('bsi,oi->bso', x, w) * s
        key = jax.random.key(seed)
        ks = jax.random.split(key, 12)
        inv = lambda fan: 1.0 / np.sqrt(fan).astype(np.float32)
        return {'x': jax.random.normal(ks[0], (4, 512, D_IN), dtype=jnp.float32), 'w1_w': _ternary(ks[1], (D_HID, D_IN)), 'w1_s': jax.random.uniform(ks[2], (D_HID,), dtype=jnp.float32) * inv(D_IN), 'w2_w': _ternary(ks[3], (D_HID, D_IN)), 'w2_s': jax.random.uniform(ks[4], (D_HID,), dtype=jnp.float32) * inv(D_IN), 'h1_w': _ternary(ks[5], (D_HID, D_HID)), 'h1_s': jax.random.uniform(ks[6], (D_HID,), dtype=jnp.float32) * inv(D_HID), 'h2_w': _ternary(ks[7], (D_HID, D_HID)), 'h2_s': jax.random.uniform(ks[8], (D_HID,), dtype=jnp.float32) * inv(D_HID), 'w3_w': _ternary(ks[9], (D_IN, D_HID)), 'w3_s': jax.random.uniform(ks[10], (D_IN,), dtype=jnp.float32) * inv(D_HID)}
    _L0_ffn_in = _L0_ffn_setup()
    _d = {'L0_attn_x': _L0_attn_in['x'], 'L0_attn_Wq': _L0_attn_in['Wq'], 'L0_attn_bq': _L0_attn_in['bq'], 'L0_attn_Wk': _L0_attn_in['Wk'], 'L0_attn_bk': _L0_attn_in['bk'], 'L0_attn_Wv': _L0_attn_in['Wv'], 'L0_attn_bv': _L0_attn_in['bv'], 'L0_attn_Wo': _L0_attn_in['Wo'], 'L0_attn_bo': _L0_attn_in['bo'], 'L0_ffn_w1_w': _L0_ffn_in['w1_w'], 'L0_ffn_w1_s': _L0_ffn_in['w1_s'], 'L0_ffn_w2_w': _L0_ffn_in['w2_w'], 'L0_ffn_w2_s': _L0_ffn_in['w2_s'], 'L0_ffn_h1_w': _L0_ffn_in['h1_w'], 'L0_ffn_h1_s': _L0_ffn_in['h1_s'], 'L0_ffn_h2_w': _L0_ffn_in['h2_w'], 'L0_ffn_h2_s': _L0_ffn_in['h2_s'], 'L0_ffn_w3_w': _L0_ffn_in['w3_w'], 'L0_ffn_w3_s': _L0_ffn_in['w3_s']}
    _x0 = _d['L0_attn_x']
    _d['L0_attn_x'] = jax.random.normal(jax.random.fold_in(jax.random.key(seed), 1), (1, 4096, 256), dtype=_x0.dtype)
    del _x0
    return _d

def reference(L0_attn_x, L0_attn_Wq, L0_attn_bq, L0_attn_Wk, L0_attn_bk, L0_attn_Wv, L0_attn_bv, L0_attn_Wo, L0_attn_bo, L0_ffn_w1_w, L0_ffn_w1_s, L0_ffn_w2_w, L0_ffn_w2_s, L0_ffn_h1_w, L0_ffn_h1_s, L0_ffn_h2_w, L0_ffn_h2_s, L0_ffn_w3_w, L0_ffn_w3_s):

    def _L0_attn_ref(x, Wq, bq, Wk, bk, Wv, bv, Wo, bo):
        import jax, jax.numpy as jnp
        import numpy as np
        import math
        N_HEAD = 16
        N_EMBD = 256
        HEAD_D = N_EMBD // N_HEAD
        BASE = 2500

        def rope(Y):
            d = Y.shape[-1]
            t = Y.shape[-2]
            theta = BASE ** (-2.0 * jnp.arange(d // 2, dtype=Y.dtype) / d)
            theta2 = jnp.concatenate([theta, theta], axis=0)
            pos = jnp.arange(1, t + 1, dtype=Y.dtype)
            C = pos[:, None] * theta2[None, :]
            cos, sin = (jnp.cos(C), jnp.sin(C))
            Y2 = jnp.concatenate([-Y[..., d // 2:], Y[..., :d // 2]], axis=-1)
            return Y * cos + Y2 * sin
        b, t, _ = x.shape

        def split_heads(y):
            return y.reshape(b, t, N_HEAD, HEAD_D).transpose(0, 2, 1, 3)
        q = split_heads(x @ Wq.T + bq)
        k = split_heads(x @ Wk.T + bk)
        v = split_heads(x @ Wv.T + bv)
        q, k = (rope(q), rope(k))
        scale = math.sqrt(HEAD_D)
        att = jnp.einsum('bhqd,bhkd->bhqk', q, k) / scale
        mask = jnp.tril(jnp.ones((t, t), dtype=bool))
        att = jnp.where(mask, att, -jnp.inf)
        att = jax.nn.softmax(att, axis=-1)
        y = jnp.einsum('bhqk,bhkd->bhqd', att, v)
        y = y.transpose(0, 2, 1, 3).reshape(b, t, N_EMBD)
        return y @ Wo.T + bo

    def _L0_ffn_ref(x, w1_w, w1_s, w2_w, w2_s, h1_w, h1_s, h2_w, h2_s, w3_w, w3_s):
        import jax, jax.numpy as jnp
        import numpy as np
        D_IN, D_HID = (256, 1024)

        def _ternary(key, shape):
            return jax.random.randint(key, shape, -1, 2).astype(jnp.float32)

        def _tlin(x, w, s):
            return jnp.einsum('bsi,oi->bso', x, w) * s
        h = jax.nn.silu(_tlin(x, w1_w, w1_s)) * _tlin(x, w2_w, w2_s)
        h = jax.nn.gelu(_tlin(h, h1_w, h1_s), approximate=False)
        h = jax.nn.gelu(_tlin(h, h2_w, h2_s), approximate=False)
        return _tlin(h, w3_w, w3_s)
    x = L0_attn_x
    x = _layernorm(x + _L0_attn_ref(x, L0_attn_Wq, L0_attn_bq, L0_attn_Wk, L0_attn_bk, L0_attn_Wv, L0_attn_bv, L0_attn_Wo, L0_attn_bo), axis=-1)
    x = _layernorm(x + _L0_ffn_ref(x, L0_ffn_w1_w, L0_ffn_w1_s, L0_ffn_w2_w, L0_ffn_w2_s, L0_ffn_h1_w, L0_ffn_h1_s, L0_ffn_h2_w, L0_ffn_h2_s, L0_ffn_w3_w, L0_ffn_w3_s), axis=-1)
    return x

_drawn_inputs = setup_inputs


def setup_inputs(seed=0):
    import zlib

    import numpy as np

    out = dict(_drawn_inputs(seed))
    spreads = {'L0_attn_bq': (0.0, 0.8),
     'L0_attn_bk': (0.0, 0.8),
     'L0_attn_bv': (0.0, 0.1),
     'L0_attn_bo': (0.0, 0.1)}
    factors = {'L0_attn_Wq': 8.0,
     'L0_attn_Wk': 8.0,
     'L0_attn_Wv': 8.0,
     'L0_ffn_w1_w': 8.0,
     'L0_ffn_w1_s': 8.0,
     'L0_ffn_w2_w': 8.0,
     'L0_ffn_w2_s': 8.0,
     'L0_ffn_h1_w': 8.0,
     'L0_ffn_h1_s': 8.0,
     'L0_ffn_h2_w': 8.0,
     'L0_ffn_h2_s': 8.0,
     'L0_ffn_w3_w': 8.0,
     'L0_ffn_w3_s': 8.0}
    for name, (base, spread) in spreads.items():
        noise = np.random.default_rng([zlib.crc32(name.encode()), seed]).standard_normal(out[name].shape)
        drawn = base * np.exp(spread * noise) if base else spread * noise
        out[name] = jnp.asarray(drawn.astype(out[name].dtype))
    for name, factor in factors.items():
        out[name] = (out[name] * factor).astype(out[name].dtype)
    return out
```

```python
import concourse.bass as bass
from concourse import mybir
from contextlib import ExitStack
import numpy as np

F32 = mybir.dt.float32
F32R = mybir.dt.float32r
BF16 = mybir.dt.bfloat16
ACT = mybir.ActivationFunctionType
ALU = mybir.AluOpType
AX = mybir.AxisListType

P = 128
T = 4096
D = 256
DH = D // P
HEADS = 16
HD = D // HEADS
CH = 512
NCH = T // CH
TPC = CH // P
NT = T // P
QUAD = 4
NQUAD = HEADS // QUAD
F = 1024
FK = F // P
VW = HD + 1
VROW = HEADS * VW + (32 - VW)
PARTS = 3
TERMS = [(0, 0), (0, 1), (1, 0), (1, 1), (0, 2), (2, 0)]
SROWS = HD * len(TERMS)
MASKED = -1e30
EPS = 1e-5


def project(nc, io, qp_d, kp_d, v_d):
    with ExitStack() as ctx:
        def sb(name, shape, dt=F32):
            return ctx.enter_context(nc.sbuf_tensor("pr_" + name, shape, dt))

        def sem(name):
            return ctx.enter_context(nc.semaphore("pr_" + name))

        wq = sb("wq", [P, DH, D])
        wk = sb("wk", [P, DH, D])
        wv = sb("wv", [P, DH, D])
        wqr = sb("wqr", [P, DH, D])
        wkr = sb("wkr", [P, DH, D])
        bias = sb("bias", [P, 4 * DH])
        sign = sb("sign", [P, 1])
        bv = sb("bv", [P, D])
        xt = sb("xt", [P, 2, DH, CH])
        cos = sb("cos", [P, 2, CH])
        sin = sb("sin", [P, 2, CH])
        t1 = sb("t1", [P, CH])
        t2 = sb("t2", [P, CH])
        full = sb("full", [P, CH])
        rest = sb("rest", [P, CH])
        parts = sb("parts", [P, 2, PARTS, CH], BF16)
        vals = sb("vals", [P, 2, 2, HEADS, VW])
        main_ps = [ctx.enter_context(nc.psum_tensor(f"pr_main{i}", [P, CH], F32)) for i in range(2)]
        rot_ps = [ctx.enter_context(nc.psum_tensor(f"pr_rot{i}", [P, CH], F32)) for i in range(2)]
        v_ps = [ctx.enter_context(nc.psum_tensor(f"pr_v{i}", [P, 2, D], F32)) for i in range(2)]

        weights_loaded = sem("weights_loaded")
        x_loaded = [sem(f"x_loaded{u}") for u in range(2)]
        tables_loaded = [sem(f"tables_loaded{u}") for u in range(2)]
        v_ones = sem("v_ones")
        weights_ready = sem("weights_ready")
        pair_ready = sem("pair_ready")
        pair_taken = sem("pair_taken")
        v_ready = sem("v_ready")
        v_taken = sem("v_taken")
        step = sem("step")
        parts_ready = sem("parts_ready")
        parts_stored = [sem(f"parts_stored{s}") for s in range(2)]
        v_stored = [sem(f"v_stored{s}") for s in range(2)]
        PAIRS = 2 * DH

        block = ctx.enter_context(nc.Block())

        @block.scalar
        def _(act):
            for dst, src in ((wq, "WqT"), (wk, "WkT"), (wv, "WvT")):
                act.dma_start(dst[:, :, :], io[src].rearrange("(c p) o -> p c o", p=P)).then_inc(weights_loaded, 16)
            act.dma_start(bias[:, :], io["bias"]).then_inc(weights_loaded, 16)
            act.dma_start(sign[:, :], io["sign"]).then_inc(weights_loaded, 16)
            act.dma_start(bv[:, :], io["bv"].partition_broadcast(P)).then_inc(weights_loaded, 16)

            def load(u, n):
                act.dma_start(xt[:, u, :, :], io["xT"][n]).then_inc(x_loaded[u], 16)
                act.dma_start(cos[:, u, :], io["cos"][n]).then_inc(tables_loaded[u], 16)
                act.dma_start(sin[:, u, :], io["sin"][n]).then_inc(tables_loaded[u], 16)

            load(0, 0)
            load(1, 1)
            with act.Fori(0, NCH // 2 - 1) as it:
                for u in range(2):
                    act.wait_ge(v_ready, it * 4 + 2 * u + 2)
                    act.wait_ge(pair_taken, it * 2 * PAIRS + PAIRS * (u + 1) + 2)
                    load(u, it * 2 + (2 + u))

        @block.gpsimd
        def _(pool):
            nc.gpsimd.memset(vals[:, :, :, :, :], 1.0).then_inc(v_ones, 1)

        @block.tensor
        def _(pe):
            pe.wait_ge(weights_ready, 6)
            with pe.Fori(0, NCH // 2) as it:
                for u in range(2):
                    pe.wait_ge(x_loaded[u], it * 16 + 16)
                    for i, (w, wr) in enumerate(((wq, wqr), (wk, wkr))):
                        for half in range(DH):
                            cols = slice(half * P, (half + 1) * P)
                            pe.wait_ge(pair_taken, it * 2 * PAIRS + PAIRS * u + DH * i + half + 1)
                            for bank, weight in ((main_ps[half], w), (rot_ps[half], wr)):
                                for c in range(DH):
                                    last = nc.tensor.matmul(bank[:, :], weight[:, c, cols], xt[:, u, c, :],
                                                            start=(c == 0), stop=(c == DH - 1))
                            last.then_inc(pair_ready, 1)
                        pe.wait_ge(v_taken, it * 4 + 2 * u + i + 1)
                        for j in range(2):
                            tile = slice((2 * i + j) * P, (2 * i + j + 1) * P)
                            for c in range(DH):
                                last = nc.tensor.matmul(v_ps[i][:, j, :], xt[:, u, c, tile], wv[:, c, :],
                                                        start=(c == 0), stop=(c == DH - 1))
                        last.then_inc(v_ready, 1)

        @block.vector
        def _(dve):
            dve.sem_inc(pair_taken, 2)
            dve.sem_inc(v_taken, 2)
            dve.wait_ge(weights_loaded, 6 * 16)
            nc.vector.tensor_scalar(wq[:, :, :], wq[:, :, :], HD ** -0.5, None, ALU.mult).then_inc(weights_ready, 1)
            nc.vector.tensor_scalar(bias[:, 0:2 * DH], bias[:, 0:2 * DH], HD ** -0.5, None,
                                    ALU.mult).then_inc(weights_ready, 1)
            dve.wait_ge(weights_ready, 2)
            for w, wr in ((wq, wqr), (wk, wkr)):
                src = w[:, :, :].rearrange("p c (h e d) -> p (c h) e d", e=2, d=HD // 2)
                dst = wr[:, :, :].rearrange("p c (h e d) -> p (c h) e d", e=2, d=HD // 2)
                nc.vector.tensor_scalar(dst[:, :, 0, :], src[:, :, 1, :], -1.0, None, ALU.mult).then_inc(weights_ready, 1)
                nc.vector.tensor_copy(dst[:, :, 1, :], src[:, :, 0, :]).then_inc(weights_ready, 1)
            for i in range(2):
                b = bias[:, (2 * i + 1) * DH:(2 * i + 2) * DH]
                nc.vector.tensor_scalar(b, b, sign[:, 0:1], None, ALU.mult).then_inc(step, 1)
            dve.wait_ge(step, 2)
            dve.wait_ge(v_ones, 1)
            with dve.Fori(0, NCH // 2) as it:
                for u in range(2):
                    dve.wait_ge(tables_loaded[u], it * 32 + 32)
                    for i in range(2):
                        for half in range(DH):
                            m = PAIRS * u + DH * i + half
                            s = half
                            b0 = 2 * DH * i + half
                            steps = it * (3 * 2 * PAIRS) + 3 * m + 2
                            dve.wait_ge(pair_ready, it * 2 * PAIRS + m + 1)
                            nc.vector.scalar_tensor_tensor(out=t1[:, :], in0=main_ps[s][:, :], scalar=bias[:, b0:b0 + 1],
                                                           in1=cos[:, u, :], op0=ALU.add, op1=ALU.mult)
                            nc.vector.scalar_tensor_tensor(out=t2[:, :], in0=rot_ps[s][:, :],
                                                           scalar=bias[:, b0 + DH:b0 + DH + 1], in1=sin[:, u, :],
                                                           op0=ALU.add, op1=ALU.mult).then_inc(pair_taken, 1)
                            dve.wait_ge(pair_taken, it * 2 * PAIRS + m + 1 + 2)
                            nc.vector.tensor_tensor(full[:, :], t1[:, :], t2[:, :], ALU.add).then_inc(step, 1)
                            dve.wait_ge(step, steps + 1)
                            dve.wait_ge(parts_stored[s], it * 192 + 48 * (2 * u + i) + 48)
                            nc.vector.tensor_copy(parts[:, s, 0, :], full[:, :]).then_inc(step, 1)
                            dve.wait_ge(step, steps + 2)
                            nc.vector.tensor_tensor(rest[:, :], full[:, :], parts[:, s, 0, :],
                                                    ALU.subtract).then_inc(step, 1)
                            dve.wait_ge(step, steps + 3)
                            nc.vector.tensor_copy(parts[:, s, 1, :], rest[:, :]).then_inc(parts_ready, 1)
                            dve.wait_ge(parts_ready, it * 4 * PAIRS + 2 * m + 1)
                            nc.vector.tensor_tensor(parts[:, s, 2, :], rest[:, :], parts[:, s, 1, :],
                                                    ALU.subtract).then_inc(parts_ready, 1)
                        dve.wait_ge(v_ready, it * 4 + 2 * u + i + 1)
                        dve.wait_ge(v_stored[i], it * 64 + 32 * u + 32)
                        for j in range(2):
                            last = nc.vector.tensor_tensor(
                                vals[:, i, j, :, 0:HD], v_ps[i][:, j, :].rearrange("p (h d) -> p h d", d=HD),
                                bv[:, :].rearrange("p (h d) -> p h d", d=HD), ALU.add)
                        last.then_inc(v_taken, 1)

        @block.sync
        def _(sp):
            for s in range(2):
                sp.sem_inc(parts_stored[s], 48)
                sp.sem_inc(v_stored[s], 32)
            with sp.Fori(0, NCH // 2) as it:
                for u in range(2):
                    for i, dst in enumerate((qp_d, kp_d)):
                        for half in range(DH):
                            m = PAIRS * u + DH * i + half
                            sp.wait_ge(parts_ready, it * 4 * PAIRS + 2 * m + 2)
                            for a in range(PARTS):
                                sp.dma_start(dst[a, half * P:(half + 1) * P, it * 2 + u, :],
                                             parts[:, half, a, :]).then_inc(parts_stored[half], 16)
                        sp.wait_ge(v_taken, it * 4 + 2 * u + i + 1 + 2)
                        for j in range(2):
                            sp.dma_start(v_d[:, :, it * 2 + u, 2 * i + j, :].rearrange("q p e -> p q e"),
                                         vals[:, i, j, :, :].rearrange("p (q h) e -> p q (h e)", q=NQUAD)
                                         ).then_inc(v_stored[i], 16)
            for s in range(2):
                sp.wait_ge(parts_stored[s], 48 * (PAIRS * NCH // 2 + 1))
                sp.wait_ge(v_stored[s], 32 * (NCH + 1))


def attend_plan():
    groups = [(c, j) for c in range(NCH) for j in range(TPC * (c + 1))]
    units = [(c, i, h, s) for c in range(NCH) for i in range(TPC) for h in range(QUAD) for s in range(c + 1)]
    lead = sum(TPC * QUAD * (c + 1) for c in range(NCH // 2))
    ahead = units[:lead]
    order = [(0, x) for x in units[lead:]] + [(1, x) for x in units[:lead]]
    return groups, units, lead, ahead, order


def spread(order, slots, total):
    work = [[] for _ in range(total)]
    for k, x in enumerate(order):
        work[k * slots // len(order)].append((k, x))
    turn, copy = [[] for _ in range(total)], [[] for _ in range(total)]
    done = 0
    for g in range(total):
        for _, (ahead, (c, i, h, s)) in work[g]:
            if (i, h, s) == (TPC - 1, QUAD - 1, c):
                turn[g + 1].append((done, ahead, c))
                copy[g + 2].append((done, ahead, c))
                done += 1
    return work, turn, copy, done


def attend(nc, io, qp_d, kp_d, v_d, max_d, o_d):
    groups, units, LEAD, ahead, order = attend_plan()
    NG = len(groups)
    NU = len(units)
    body_work, body_turn, body_copy, body_done = spread(order, NG - 4, NG)
    pre_work, pre_turn, pre_copy, pre_done = spread([(0, x) for x in ahead], LEAD // 4, LEAD // 4 + 3)
    RING_S = 3
    RING_P = 3
    MR = PARTS * QUAD * TPC
    with ExitStack() as ctx:
        def sb(name, shape, dt=F32):
            return ctx.enter_context(nc.sbuf_tensor("at_" + name, shape, dt))

        def sem(name):
            return ctx.enter_context(nc.semaphore("at_" + name))

        qst = [sb(f"q_stack{u}", [P, NCH, QUAD, CH], BF16) for u in range(2)]
        kst = [sb(f"k_stack{u}", [P, QUAD, T], BF16) for u in range(2)]
        vq = [sb(f"values{u}", [P, NT * QUAD * VW + 32 - VW]) for u in range(2)]
        probs = sb("probs", [P, RING_P, QUAD, CH])
        outs = sb("outs", [P, 2, CH])
        ident32 = sb("ident32", [P, P])
        mask32 = sb("mask32", [P, P])
        ident = sb("ident", [P, P], BF16)
        mask = sb("mask", [P, P], BF16)
        segmax = sb("segmax", [P, QUAD * TPC, NCH])
        negmax = sb("negmax", [P, QUAD * TPC])
        maxrest = sb("maxrest", [P, QUAD * TPC])
        maxparts = sb("maxparts", [P, PARTS, QUAD * TPC], BF16)
        maxrows = sb("maxrows", [MR, NCH, P], BF16)
        row_ps = [ctx.enter_context(nc.psum_tensor(f"at_row{i}", [P, CH], F32)) for i in range(RING_S)]
        key_ps = [ctx.enter_context(nc.psum_tensor(f"at_key{i}", [P, CH], F32)) for i in range(RING_S)]
        o_ps = ctx.enter_context(nc.psum_tensor("at_o", [P, CH], F32))
        turn_ps = ctx.enter_context(nc.psum_tensor("at_turn", [P, P], F32))

        consts_loaded = sem("consts_loaded")
        consts_ready = sem("consts_ready")
        ones_ready = sem("ones_ready")
        stacks_loaded = [sem(f"stacks_loaded{u}") for u in range(2)]
        values_loaded = [sem(f"values_loaded{u}") for u in range(2)]
        rows_ready = sem("rows_ready")
        rows_taken = sem("rows_taken")
        split = sem("split")
        maxparts_ready = sem("maxparts_ready")
        turned = sem("turned")
        maxrows_ready = sem("maxrows_ready")
        max_spilled = sem("max_spilled")
        max_stored = [sem(f"max_stored{c}") for c in range(NCH)]
        keys_ready = sem("keys_ready")
        probs_ready = sem("probs_ready")
        probs_used = sem("probs_used")
        out_taken = sem("out_taken")
        out_stored = sem("out_stored")
        out_free = sem("out_free")
        STACK_INC = (QUAD + 1) * len(TERMS) * 16

        block = ctx.enter_context(nc.Block())

        @block.gpsimd
        def _(pool):
            def load(u, quad):
                q_v = qp_d.rearrange("a (q h d) n t -> a q d h n t", q=NQUAD, d=HD)
                k_v = kp_d.rearrange("a (q h d) n t -> a q d h (n t)", q=NQUAD, d=HD)
                for r, (qa, ka) in enumerate(TERMS):
                    rows = slice(r * HD, (r + 1) * HD)
                    for h in range(QUAD):
                        pool.dma_start(qst[u][rows, :, h, :], q_v[qa, quad, :, h]).then_inc(stacks_loaded[u], 16)
                    pool.dma_start(kst[u][rows, :, :], k_v[ka, quad]).then_inc(stacks_loaded[u], 16)
                pool.dma_start(vq[u][:, 0:NT * QUAD * VW], v_d[quad].rearrange("p n i e -> p (n i e)")
                               ).then_inc(values_loaded[u], 16)

            def store(quad, c, count):
                pool.wait_ge(out_taken, count + 2)
                pool.dma_start(o_d[c, quad, :, :], outs[:, c % 2, :]).then_inc(out_stored, 16)
                pool.wait_ge(out_stored, count * 16 + 16)
                pool.sem_inc(out_free, 1)

            load(0, 0)
            for u in range(2):
                nc.gpsimd.memset(kst[u][SROWS:SROWS + PARTS, :, :], 1.0).then_inc(ones_ready, 1)
                pool.wait_ge(ones_ready, 2 * u + 1)
                nc.gpsimd.memset(vq[u][:, NT * QUAD * VW:], 0.0).then_inc(ones_ready, 1)
                pool.wait_ge(ones_ready, 2 * u + 2)
            pool.sem_inc(out_free, 2)
            with pool.Fori(0, NQUAD // 2) as it:
                pool.wait_ge(probs_used, it * 2 * NG + RING_P)
                load(1, it * 2 + 1)
                for c in range(NCH):
                    store(it * 2, c, it * 2 * NCH + c)
                pool.wait_ge(probs_used, it * 2 * NG + NG + RING_P)
                load(0, it * (-2) + 2)
                for c in range(NCH):
                    store(it * 2 + 1, c, it * 2 * NCH + NCH + c)
            pool.wait_ge(values_loaded[0], 16 * (NQUAD // 2 + 1))

        @block.sync
        def _(sp):
            sp.dma_start(ident32[:, :], io["ident"]).then_inc(consts_loaded, 16)
            sp.dma_start(mask32[:, :], io["mask"]).then_inc(consts_loaded, 16)

            def store_max(u, c, count):
                sp.wait_ge(maxrows_ready, count + 2)
                sp.dma_start(max_d[c].rearrange("a (r x) -> (a r) x", x=P), maxrows[:, c, :]).then_inc(max_spilled, 16)
                sp.wait_ge(max_spilled, count * 16 + 16)
                sp.dma_start(qst[u][SROWS:SROWS + PARTS, c, :, :].rearrange("a h t -> a (h t)"), max_d[c]
                             ).then_inc(max_stored[c], 16)

            for g in pre_turn:
                for n, _, c in g:
                    store_max(0, c, n)
            with sp.Fori(0, NQUAD // 2) as it:
                for u in range(2):
                    for g in body_turn:
                        for n, hence, c in g:
                            store_max((u + hence) % 2, c, it * 2 * body_done + u * body_done + pre_done + n)
            for c in range(NCH // 2):
                sp.wait_ge(max_stored[c], 16 * (NQUAD + 1))
            for c in range(NCH // 2, NCH):
                sp.wait_ge(max_stored[c], 16 * NQUAD)

        @block.tensor
        def _(pe):
            def row_unit(u, c, i, h, s, count, slot):
                w = CH if s < c else (i + 1) * P
                bank = row_ps[slot]
                pe.wait_ge(rows_taken, count + 1)
                last = nc.tensor.matmul(bank[:, 0:w], qst[u][0:SROWS, c, h, i * P:(i + 1) * P],
                                        kst[u][0:SROWS, h, s * CH:s * CH + w], start=True, stop=(s < c))
                if s == c:
                    last = nc.tensor.matmul(bank[:, w - P:w], mask[:, :], ident[:, :], start=False, stop=True)
                last.then_inc(rows_ready, 1)

            def turn(count):
                pe.wait_ge(maxparts_ready, count + 1)
                pe.wait_ge(maxrows_ready, count + 1)
                nc.tensor.matmul(turn_ps[0:MR, :], maxparts[:, :, :].rearrange("p a r -> p (a r)"), ident[:, :], start=True, stop=True
                                 ).then_inc(turned, 1)

            def key_unit(u, c, j, h, count, slot):
                q0 = max(0, j * P - c * CH)
                bank = key_ps[slot]
                pe.wait_ge(probs_ready, count + 1)
                last = nc.tensor.matmul(bank[:, q0:CH], kst[u][0:SROWS + PARTS, h, j * P:(j + 1) * P],
                                        qst[u][0:SROWS + PARTS, c, h, q0:CH],
                                        start=True, stop=(j < TPC * c))
                if j >= TPC * c:
                    last = nc.tensor.matmul(bank[:, q0:q0 + P], ident[:, :], mask[:, :], start=False, stop=True)
                last.then_inc(keys_ready, 1)

            def values(u, g, quad, first):
                c, j = groups[g]
                q0 = max(0, j * P - c * CH)
                last_j = j == TPC * (c + 1) - 1
                if j == 0:
                    pe.wait_ge(out_taken, quad * NCH + c + 1)
                pe.wait_ge(probs_ready, first + QUAD * (g + 1) + RING_S)
                for h in range(QUAD):
                    at = j * QUAD * VW + h * VW
                    last = nc.tensor.matmul(o_ps[32 * h:32 * h + 32, q0:CH], vq[u][:, at:at + 32],
                                            probs[:, g % RING_P, h, q0:CH], start=(j == 0), stop=last_j)
                last.then_inc(probs_used, 1)

            pe.sem_inc(probs_used, RING_P)
            pe.wait_ge(consts_ready, 2)
            pe.wait_ge(stacks_loaded[0], STACK_INC)
            for g in range(len(pre_work)):
                for k, (_, x) in pre_work[g]:
                    row_unit(0, *x, k, k % RING_S)
                for n, _, _ in pre_turn[g]:
                    turn(n)
            pe.wait_ge(ones_ready, 4)
            rows_before = pe.alloc_register("rows_before")
            with pe.Fori(0, NQUAD // 2) as it:
                for u in range(2):
                    quad = it * 2 + u
                    first = pe.snap(it * 2 * NU + u * NU)
                    pe.reg_mov(rows_before, it * 2 * NU + (u * NU + LEAD))
                    first_row = pe.snap(rows_before)
                    waited = False
                    for g, (c, j) in enumerate(groups):
                        if j == 0:
                            pe.wait_ge(max_stored[c], quad * 16 + 16)
                        row = list(body_work[g])
                        for h in range(QUAD):
                            while row and len(row) >= QUAD - h:
                                k, (hence, x) = row.pop(0)
                                if hence and not waited:
                                    pe.wait_ge(stacks_loaded[1 - u], it * STACK_INC + (u + 1) * STACK_INC)
                                    waited = True
                                row_unit((u + hence) % 2, *x, first_row + k, (LEAD + k) % RING_S)
                            key_unit(u, c, j, h, first + QUAD * g + h, (QUAD * g + h) % RING_S)
                        if g == 1:
                            pe.wait_ge(values_loaded[u], it * 16 + 16)
                        if g >= 1:
                            values(u, g - 1, quad, first)
                        for n, _, _ in body_turn[g]:
                            turn(it * 2 * body_done + u * body_done + pre_done + n)
                    values(u, NG - 1, quad, first)

        @block.vector
        def _(dve):
            def segment(c, i, h, s, count, slot):
                w = CH if s < c else (i + 1) * P
                r = h * TPC + i
                dve.wait_ge(rows_ready, count + 1)
                nc.vector.tensor_reduce(segmax[:, r, s:s + 1], row_ps[slot][:, 0:w], op=ALU.max, axis=AX.X
                                        ).then_inc(rows_taken, 1)

            def finish(c, units_done, count):
                dve.wait_ge(rows_taken, units_done + RING_S)
                nc.vector.tensor_reduce(negmax[:, :], segmax[:, :, 0:c + 1], op=ALU.max, axis=AX.X, negate=True
                                        ).then_inc(split, 1)
                dve.wait_ge(split, count * 4 + 1)
                nc.vector.tensor_copy(maxparts[:, 0, :], negmax[:, :]).then_inc(split, 1)
                dve.wait_ge(split, count * 4 + 2)
                nc.vector.tensor_tensor(maxrest[:, :], negmax[:, :], maxparts[:, 0, :], ALU.subtract).then_inc(split, 1)
                dve.wait_ge(split, count * 4 + 3)
                nc.vector.tensor_copy(maxparts[:, 1, :], maxrest[:, :]).then_inc(split, 1)
                dve.wait_ge(split, count * 4 + 4)
                nc.vector.tensor_tensor(maxparts[:, 2, :], maxrest[:, :], maxparts[:, 1, :], ALU.subtract
                                        ).then_inc(maxparts_ready, 1)

            def copy_rows(c, count):
                dve.wait_ge(turned, count + 1)
                nc.vector.tensor_copy(maxrows[:, c, :], turn_ps[0:MR, :]).then_inc(maxrows_ready, 1)

            dve.wait_ge(consts_loaded, 32)
            nc.vector.tensor_copy(ident[:, :], ident32[:, :]).then_inc(consts_ready, 1)
            nc.vector.tensor_copy(mask[:, :], mask32[:, :]).then_inc(consts_ready, 1)
            dve.sem_inc(rows_taken, RING_S)
            dve.sem_inc(maxrows_ready, 1)
            done = 0
            for g in range(len(pre_work)):
                for k, (_, (c, i, h, s)) in pre_work[g]:
                    segment(c, i, h, s, k, k % RING_S)
                    if (i, h, s) == (TPC - 1, QUAD - 1, c):
                        finish(c, k + 1, done)
                        done += 1
                for n, _, c in pre_copy[g]:
                    copy_rows(c, n)
            with dve.Fori(0, NQUAD // 2) as it:
                for u in range(2):
                    k0 = it * 2 * NU + (u * NU + LEAD)
                    n0 = it * 2 * body_done + (u * body_done + pre_done)
                    done = 0
                    for g in range(NG):
                        for k, (_, (c, i, h, s)) in body_work[g]:
                            segment(c, i, h, s, k0 + k, (LEAD + k) % RING_S)
                            if (i, h, s) == (TPC - 1, QUAD - 1, c):
                                finish(c, k0 + k + 1, n0 + done)
                                done += 1
                        for n, _, c in body_copy[g]:
                            copy_rows(c, n0 + n)

        @block.scalar
        def _(act):
            act.sem_inc(probs_ready, RING_S)
            act.sem_inc(out_taken, 1)
            with act.Fori(0, NQUAD // 2) as it:
                for u in range(2):
                    g0 = it * 2 * NG + u * NG
                    first = it * 2 * NU + u * NU
                    quad = it * 2 + u

                    def take_out(c):
                        last_g = TPC * (c + 1) * (c + 2) // 2 - 1
                        act.wait_ge(probs_used, g0 + last_g + 1 + RING_P)
                        act.wait_ge(out_free, quad * NCH + c + 1)
                        nc.scalar.activation(outs[:, c % 2, :], o_ps[:, :], ACT.Copy).then_inc(out_taken, 1)

                    for g, (c, j) in enumerate(groups):
                        q0 = max(0, j * P - c * CH)
                        act.wait_ge(probs_used, g0 + g + 1)
                        for h in range(QUAD):
                            act.wait_ge(keys_ready, first + QUAD * g + h + 1)
                            nc.scalar.activation(probs[:, g % RING_P, h, q0:CH],
                                                 key_ps[(QUAD * g + h) % RING_S][:, q0:CH], ACT.Exp
                                                 ).then_inc(probs_ready, 1)
                            if h == 0 and c > 0 and j == 1:
                                take_out(c - 1)
                    take_out(NCH - 1)


def widen(nc, io, o_d, x1_d, h2_d):
    with ExitStack() as ctx:
        def sb(name, shape, dt=F32):
            return ctx.enter_context(nc.sbuf_tensor("wi_" + name, shape, dt))

        def sem(name):
            return ctx.enter_context(nc.semaphore("wi_" + name))

        w1 = [sb(f"w1_{a}", [P, DH, F], F32R) for a in "hl"]
        w2 = [sb(f"w2_{a}", [P, DH, F], F32R) for a in "hl"]
        h1w = [sb(f"h1w_{a}", [P, FK, F], F32R) for a in "hl"]
        wo = sb("wo", [P, NQUAD, D])
        spread_den = sb("spread_den", [P, P])
        ident = sb("ident", [P, P])
        stage = sb("stage", [P, 2, F])
        bo = sb("bo", [P, D])
        s1 = sb("s1", [P, FK])
        s2 = sb("s2", [P, FK])
        hs = sb("hs", [P, FK])
        o = sb("o", [P, 2, NQUAD, CH])
        x = sb("x", [P, 2, TPC, D])
        recip = sb("recip", [P, 2, CH])
        x1 = sb("x1", [P, TPC, D])
        stats = sb("stats", [P, TPC, 6])
        mv = sb("mv", [P, TPC, 2])
        var = sb("var", [P, TPC])
        power = sb("power", [P, TPC])
        rstd = sb("rstd", [P, TPC])
        x1t = [sb(f"x1t_{a}", [P, 2, DH, CH], F32R) for a in "hl"]
        silu = sb("silu", [P, 2, CH])
        gated = sb("gated", [P, 2, CH])
        h1 = [sb(f"h1_{a}", [P, FK, CH], F32R) for a in "hl"]
        h2 = sb("h2", [P, 2, CH])
        fb = [ctx.enter_context(nc.psum_tensor(f"wi_f{i}", [P, CH], F32)) for i in range(4)]
        pb = [ctx.enter_context(nc.psum_tensor(f"wi_p{i}", [P, CH], F32)) for i in range(2)]

        consts_loaded = sem("consts_loaded")
        wo_zero = sem("wo_zero")
        staged = [sem(f"staged{s}") for s in range(2)]
        weight_split = sem("weight_split")
        power_ready = sem("power_ready")
        o_loaded = [sem(f"o_loaded{u}") for u in range(2)]
        x_loaded = [sem(f"x_loaded{u}") for u in range(2)]
        den_ready = sem("den_ready")
        den_taken = sem("den_taken")
        y_ready = sem("y_ready")
        proj_ready = sem("proj_ready")
        step = sem("step")
        stats_passed = sem("stats_passed")
        var_ready = sem("var_ready")
        rstd_ready = sem("rstd_ready")
        x1_ready = sem("x1_ready")
        x1_stored = sem("x1_stored")
        turned = sem("turned")
        x1t_high = sem("x1t_high")
        x1t_ready = sem("x1t_ready")
        pair_ready = sem("pair_ready")
        silu_ready = sem("silu_ready")
        pair_taken = sem("pair_taken")
        h1_high = sem("h1_high")
        h1_ready = sem("h1_ready")
        hid_ready = sem("hid_ready")
        hid_taken = sem("hid_taken")
        h2_stored = [sem(f"h2_stored{s}") for s in range(2)]

        NORM = 4
        pieces = []
        for name, w, n in (("w1T", w1, DH), ("w2T", w2, DH), ("h1T", h1w, FK)):
            pieces += [(name, k, w[0][:, k, :], w[1][:, k, :]) for k in range(n)]
        NPIECE = len(pieces)

        block = ctx.enter_context(nc.Block())

        def chunks(engine, body):
            with engine.Fori(0, NCH // 2 - 1) as it:
                for u in range(2):
                    body(it * 2 + u, u, True, True)
            body(NCH - 2, 0, True, False)
            body(NCH - 1, 1, False, False)

        def o_count(m, u):
            return (m + (2 - u)) * 8

        @block.gpsimd
        def _(pool):
            nc.gpsimd.memset(wo[:, :, :], 0.0).then_inc(wo_zero, 1)
            nc.gpsimd.memset(power[:, :], -0.5).then_inc(power_ready, 1)
            pool.wait_ge(power_ready, 1)

            def inverse_root(m):
                pool.wait_ge(var_ready, m + 1)
                nc.gpsimd.tensor_tensor(rstd[:, :], var[:, :], power[:, :], ALU.pow).then_inc(rstd_ready, 1)

            inverse_root(0)
            with pool.Fori(0, NCH - 1) as n:
                inverse_root(n + 1)

        @block.sync
        def _(sp):
            sp.dma_start(spread_den[:, :], io["spread"]).then_inc(consts_loaded, 16)
            sp.dma_start(ident[:, :], io["ident"]).then_inc(consts_loaded, 16)
            sp.dma_start(bo[:, :], io["bo"].partition_broadcast(P)).then_inc(consts_loaded, 16)
            for dst, src in ((s1, "s1"), (s2, "s2"), (hs, "hs1")):
                sp.dma_start(dst[:, :], io[src]).then_inc(consts_loaded, 16)
            sp.wait_ge(wo_zero, 1)
            for h in range(QUAD):
                sp.dma_start(wo[32 * h:32 * h + HD, :, :],
                             io["WoT"].rearrange("(q h d) o -> h d q o", q=NQUAD, d=HD)[h]).then_inc(consts_loaded, 16)

            def load(n, u):
                sp.dma_start(o[:, u, :, :], o_d[n].rearrange("q p t -> p q t")).then_inc(o_loaded[u], 16)
                sp.dma_start(x[:, u, :, :], io["x"].rearrange("(n i p) d -> n p i d", i=TPC, p=P)[n]
                             ).then_inc(x_loaded[u], 16)

            load(0, 0)
            load(1, 1)

            def store_x1(m):
                sp.wait_ge(x1_ready, m * TPC + TPC)
                sp.dma_start(x1_d[m], x1[:, :, :]).then_inc(x1_stored, 16)

            sp.sem_inc(x1_stored, 16)
            for s in range(2):
                sp.sem_inc(h2_stored[s], 16)
            store_x1(0)

            def body(n, u, prepare, fetch):
                if fetch:
                    load(n + 2, u)
                for k in range(FK):
                    if k == FK - 1 and prepare:
                        store_x1(n + 1)
                    sp.wait_ge(hid_taken, n * FK + (k + 1 + FK))
                    sp.dma_start(h2_d[n, :, k, :], h2[:, k % 2, :]).then_inc(h2_stored[k % 2], 16)

            chunks(sp, body)
            for s in range(2):
                sp.wait_ge(h2_stored[s], 16 * (NCH * FK // 2 + 1))
            sp.wait_ge(x1_stored, 16 * (NCH + 1))

        @block.tensor
        def _(pe):
            def prepare_den(m, u, q):
                if q == 0:
                    pe.wait_ge(o_loaded[u], o_count(m, u))
                if q < 2:
                    pe.wait_ge(x1t_ready, m * 2 + q + 1)
                else:
                    pe.wait_ge(den_taken, m * NQUAD + q - 1)
                nc.tensor.matmul(pb[q % 2][:, :], spread_den[:, :], o[:, u, q, :], start=True, stop=True
                                 ).then_inc(den_ready, 1)

            def prepare_proj(m, u):
                for b in range(2):
                    pe.wait_ge(y_ready, m * NQUAD + NQUAD)
                    for j in range(2):
                        tile = slice((2 * b + j) * P, (2 * b + j + 1) * P)
                        for q in range(NQUAD):
                            last = nc.tensor.matmul(pb[b][:, j * D:(j + 1) * D], o[:, u, q, tile], wo[:, q, :],
                                                    start=(q == 0), stop=(q == NQUAD - 1))
                    last.then_inc(proj_ready, 1)

            def prepare_turn(m, u):
                pe.wait_ge(x1_ready, m * TPC + TPC)
                for c in range(DH):
                    for i in range(TPC):
                        last = nc.tensor.transpose(pb[c][:, i * P:(i + 1) * P], x1[:, i, c * P:(c + 1) * P], ident[:, :])
                    last.then_inc(turned, 1)

            def product(bank, w, act_in, pieces_k, cols):
                n = 0
                for k in range(pieces_k):
                    for a, b in ((0, 0), (0, 1), (1, 0)):
                        last = nc.tensor.matmul(bank[:, :], w[a][:, k, cols], act_in[b](k),
                                                start=(n == 0), stop=(n == 3 * pieces_k - 1))
                        n += 1
                return last

            def body(n, u, prepare, fetch):
                pe.wait_ge(x1t_ready, n * 2 + 4)
                for k in range(FK):
                    cols = slice(k * P, (k + 1) * P)
                    if k < 2:
                        pe.wait_ge(hid_taken, n * FK + (6 + 2 * k))
                    else:
                        pe.wait_ge(pair_taken, n * FK + (k - 1))
                    for j, w in ((0, w1), (1, w2)):
                        xs = [lambda c, a=a: x1t[a][:, u, c, :] for a in range(2)]
                        last = product(fb[2 * (k % 2) + j], w, xs, DH, cols)
                    last.then_inc(pair_ready, 1)
                if prepare:
                    prepare_den(n + 1, 1 - u, 0)
                    prepare_den(n + 1, 1 - u, 1)
                for k in range(FK):
                    if prepare and k == 2:
                        prepare_den(n + 1, 1 - u, 2)
                        prepare_den(n + 1, 1 - u, 3)
                    if prepare and k == 5:
                        prepare_proj(n + 1, 1 - u)
                    if prepare and k == 7:
                        prepare_turn(n + 1, 1 - u)
                    if k == 0:
                        pe.wait_ge(h1_ready, n * FK + FK)
                    if k < 4:
                        pe.wait_ge(pair_taken, n * FK + (7 + k // 2))
                    else:
                        pe.wait_ge(hid_taken, n * FK + (k - 3 + FK))
                    hsrc = [lambda c, a=a: h1[a][:, c, :] for a in range(2)]
                    product(fb[k % 4], h1w, hsrc, FK, slice(k * P, (k + 1) * P)).then_inc(hid_ready, 1)

            pe.wait_ge(consts_loaded, 16 * (6 + QUAD))
            for q in range(NQUAD):
                prepare_den(0, 0, q)
            prepare_proj(0, 0)
            prepare_turn(0, 0)
            pe.wait_ge(weight_split, 2 * NPIECE)
            chunks(pe, body)

        @block.scalar
        def _(act):
            for p, (name, k, _, _) in enumerate(pieces):
                if p >= 2:
                    act.wait_ge(weight_split, 2 * (p - 1))
                act.dma_start(stage[:, p % 2, :], io[name][k * P:(k + 1) * P, :]).then_inc(staged[p % 2], 16)
            act.sem_inc(hid_taken, FK)
            act.wait_ge(consts_loaded, 16 * (6 + QUAD))

            def body(n, u, prepare, fetch):
                for k in range(FK):
                    act.wait_ge(pair_ready, n * FK + (k + 1))
                    nc.scalar.activation(silu[:, k % 2, :], fb[2 * (k % 2)][:, :], ACT.Silu, scale=s1[:, k:k + 1]
                                         ).then_inc(silu_ready, 1)
                for k in range(FK):
                    act.wait_ge(hid_ready, n * FK + (k + 1))
                    act.wait_ge(h2_stored[k % 2], n * 64 + (16 * (k // 2) + 16))
                    nc.scalar.activation(h2[:, k % 2, :], fb[k % 4][:, :], ACT.Gelu, scale=hs[:, k:k + 1]
                                         ).then_inc(hid_taken, 1)

            chunks(act, body)

        @block.vector
        def _(dve):
            dve.sem_inc(x1t_ready, 2)
            dve.wait_ge(consts_loaded, 16 * (6 + QUAD))

            def prepare_y(m, u):
                dve.wait_ge(o_loaded[u], o_count(m, u))
                for q in range(NQUAD):
                    dve.wait_ge(den_ready, m * NQUAD + (q + 1))
                    nc.vector.reciprocal(recip[:, q % 2, :], pb[q % 2][:, :]).then_inc(den_taken, 1)
                    dve.wait_ge(den_taken, m * NQUAD + (q + 1))
                    nc.vector.tensor_tensor(o[:, u, q, :], o[:, u, q, :], recip[:, q % 2, :], ALU.mult
                                            ).then_inc(y_ready, 1)

            def prepare_norm(m, u):
                dve.wait_ge(x_loaded[u], o_count(m, u))
                dve.wait_ge(x1_stored, m * 16 + 16)
                if not (isinstance(m, int) and m == 0):
                    dve.wait_ge(turned, m * 2)
                for i in range(TPC):
                    if i % 2 == 0:
                        dve.wait_ge(proj_ready, m * 2 + (i // 2 + 1))
                    last = nc.vector.tensor_tensor(x1[:, i, :], pb[i // 2][:, (i % 2) * D:(i % 2 + 1) * D], bo[:, :],
                                                   ALU.add)
                last.then_inc(step, 1)
                dve.wait_ge(step, m * NORM + 1)
                nc.vector.tensor_tensor(x1[:, :, :], x1[:, :, :], x[:, u, :, :], ALU.add).then_inc(step, 1)
                dve.wait_ge(step, m * NORM + 2)
                for i in range(TPC):
                    last = nc.vector.bn_stats(stats[:, i, :], x1[:, i, :])
                last.then_inc(step, 1)
                dve.wait_ge(step, m * NORM + 3)
                dve.sem_inc(stats_passed, 1)
                for i in range(TPC):
                    last = nc.vector.bn_aggr(mv[:, i, :], stats[:, i, :])
                last.then_inc(step, 1)
                dve.wait_ge(step, m * NORM + 4)
                nc.vector.tensor_scalar(var[:, :], mv[:, :, 1], EPS, None, ALU.add).then_inc(var_ready, 1)
                dve.wait_ge(rstd_ready, m + 1)
                for i in range(TPC):
                    nc.vector.tensor_scalar(x1[:, i, :], x1[:, i, :], mv[:, i, 0:1], rstd[:, i:i + 1],
                                            ALU.subtract, ALU.mult).then_inc(x1_ready, 1)

            def prepare_x1t(m, u):
                for c in range(DH):
                    dve.wait_ge(turned, m * 2 + (c + 1))
                    nc.vector.tensor_copy(x1t[0][:, u, c, :], pb[c][:, :]).then_inc(x1t_high, 1)
                    dve.wait_ge(x1t_high, m * 2 + (c + 1))
                    nc.vector.tensor_tensor(x1t[1][:, u, c, :], pb[c][:, :], x1t[0][:, u, c, :].bitcast(F32),
                                            ALU.subtract).then_inc(x1t_ready, 1)

            def body(n, u, prepare, fetch):
                for k in range(FK):
                    dve.wait_ge(silu_ready, n * FK + (k + 1))
                    nc.vector.scalar_tensor_tensor(out=gated[:, k % 2, :], in0=fb[2 * (k % 2) + 1][:, :],
                                                   scalar=s2[:, k:k + 1], in1=silu[:, k % 2, :],
                                                   op0=ALU.mult, op1=ALU.mult).then_inc(pair_taken, 1)
                    dve.wait_ge(pair_taken, n * FK + (k + 1))
                    nc.vector.tensor_copy(h1[0][:, k, :], gated[:, k % 2, :]).then_inc(h1_high, 1)
                    dve.wait_ge(h1_high, n * FK + (k + 1))
                    nc.vector.tensor_tensor(h1[1][:, k, :], gated[:, k % 2, :], h1[0][:, k, :].bitcast(F32), ALU.subtract
                                            ).then_inc(h1_ready, 1)
                if prepare:
                    prepare_y(n + 1, 1 - u)
                    prepare_norm(n + 1, 1 - u)
                    prepare_x1t(n + 1, 1 - u)

            prepare_y(0, 0)
            prepare_norm(0, 0)
            prepare_x1t(0, 0)
            for p, (name, k, high, low) in enumerate(pieces):
                dve.wait_ge(staged[p % 2], 16 * (p // 2 + 1))
                nc.vector.tensor_copy(high, stage[:, p % 2, :]).then_inc(weight_split, 1)
                dve.wait_ge(weight_split, 2 * p + 1)
                nc.vector.tensor_tensor(low, stage[:, p % 2, :], high.bitcast(F32), ALU.subtract
                                        ).then_inc(weight_split, 1)
            chunks(dve, body)


def narrow(nc, io, x1_d, h2_d, out):
    with ExitStack() as ctx:
        def sb(name, shape, dt=F32):
            return ctx.enter_context(nc.sbuf_tensor("na_" + name, shape, dt))

        def sem(name):
            return ctx.enter_context(nc.semaphore("na_" + name))

        h2w = [sb(f"h2w_{a}", [P, FK, F], F32R) for a in "hl"]
        w3 = [sb(f"w3_{a}", [P, FK, D], F32R) for a in "hl"]
        stage = sb("stage", [P, 2, F])
        hs = sb("hs", [P, FK])
        s3 = sb("s3", [P, D])
        h2f = sb("h2f", [P, 2, FK, CH])
        h2 = [sb(f"h2_{a}", [P, FK, CH], F32R) for a in "hl"]
        h3f = sb("h3f", [P, 2, CH])
        h3 = [sb(f"h3_{a}", [P, FK, CH], F32R) for a in "hl"]
        x1 = sb("x1", [P, TPC, D])
        y = sb("y", [P, TPC, D])
        stats = sb("stats", [P, TPC, 6])
        mv = sb("mv", [P, TPC, 2])
        var = sb("var", [P, TPC])
        power = sb("power", [P, TPC])
        rstd = sb("rstd", [P, TPC])
        hb = [ctx.enter_context(nc.psum_tensor(f"na_h{i}", [P, CH], F32)) for i in range(4)]
        yb = [ctx.enter_context(nc.psum_tensor(f"na_y{i}", [P, CH], F32)) for i in range(2)]

        consts_loaded = sem("consts_loaded")
        staged = [sem(f"staged{s}") for s in range(2)]
        weight_split = sem("weight_split")
        power_ready = sem("power_ready")
        h2_loaded = [sem(f"h2_loaded{u}") for u in range(2)]
        x1_loaded = sem("x1_loaded")
        h2_high = sem("h2_high")
        h2_ready = sem("h2_ready")
        hid_ready = sem("hid_ready")
        hid_taken = sem("hid_taken")
        h3_high = sem("h3_high")
        h3_ready = sem("h3_ready")
        y_ready = sem("y_ready")
        y_scaled = sem("y_scaled")
        step = sem("step")
        stats_passed = sem("stats_passed")
        var_ready = sem("var_ready")
        rstd_ready = sem("rstd_ready")
        out_ready = sem("out_ready")
        out_stored = sem("out_stored")

        NORM = 3
        pieces = [("h2T", k, h2w[0][:, k, :], h2w[1][:, k, :]) for k in range(FK)]
        pieces += [("w3T", g, w3[0][:, 4 * g:4 * g + 4, :], w3[1][:, 4 * g:4 * g + 4, :]) for g in range(FK // 4)]
        NPIECE = len(pieces)

        block = ctx.enter_context(nc.Block())

        def chunks(engine, body):
            with engine.Fori(0, NCH // 2 - 1) as it:
                for u in range(2):
                    body(it * 2 + u, u, True, True)
            body(NCH - 2, 0, True, False)
            body(NCH - 1, 1, False, False)

        def h2_count(m, u):
            return (m + (2 - u)) * 8

        @block.gpsimd
        def _(pool):
            nc.gpsimd.memset(power[:, :], -0.5).then_inc(power_ready, 1)
            pool.wait_ge(power_ready, 1)
            with pool.Fori(0, NCH) as n:
                pool.wait_ge(var_ready, n + 1)
                nc.gpsimd.tensor_tensor(rstd[:, :], var[:, :], power[:, :], ALU.pow).then_inc(rstd_ready, 1)

        @block.sync
        def _(sp):
            sp.dma_start(hs[:, :], io["hs2"]).then_inc(consts_loaded, 16)
            sp.dma_start(s3[:, :], io["s3"].partition_broadcast(P)).then_inc(consts_loaded, 16)

            def load_h2(n, u):
                sp.dma_start(h2f[:, u, :, :], h2_d[n]).then_inc(h2_loaded[u], 16)

            load_h2(0, 0)
            load_h2(1, 1)
            sp.dma_start(x1[:, :, :], x1_d[0]).then_inc(x1_loaded, 16)
            sp.sem_inc(out_stored, 16)

            def body(n, u, prepare, fetch):
                if fetch:
                    sp.wait_ge(h2_ready, n * FK + FK)
                    load_h2(n + 2, u)
                if prepare:
                    sp.wait_ge(y_scaled, n + 1)
                    sp.dma_start(x1[:, :, :], x1_d[n + 1]).then_inc(x1_loaded, 16)
                sp.wait_ge(out_ready, n * TPC + TPC)
                sp.dma_start(out.rearrange("(n i p) d -> n p i d", i=TPC, p=P)[n], y[:, :, :]).then_inc(out_stored, 16)

            chunks(sp, body)
            sp.wait_ge(out_stored, 16 * (NCH + 1))

        @block.tensor
        def _(pe):
            pe.wait_ge(weight_split, 2 * FK)
            pe.sem_inc(y_ready, 2)
            pe.sem_inc(hid_ready, FK)

            def body(n, u, prepare, fetch):
                for k in range(FK):
                    if k == 0:
                        pe.wait_ge(h2_ready, n * FK + FK)
                    pe.wait_ge(hid_taken, n * FK + (k + 1))
                    cols = slice(k * P, (k + 1) * P)
                    m = 0
                    for c in range(FK):
                        for a, b in ((0, 0), (0, 1), (1, 0)):
                            last = nc.tensor.matmul(hb[k % 4][:, :], h2w[a][:, c, cols], h2[b][:, c, :],
                                                    start=(m == 0), stop=(m == 3 * FK - 1))
                            m += 1
                    last.then_inc(hid_ready, 1)
                pe.wait_ge(weight_split, 2 * NPIECE)
                for i in range(TPC):
                    tile = slice(i * P, (i + 1) * P)
                    m = 0
                    for c in range(FK):
                        if i == 0:
                            pe.wait_ge(h3_ready, n * FK + (c + 1 + 2))
                        for a, b in ((0, 0), (0, 1), (1, 0)):
                            last = nc.tensor.matmul(yb[i // 2][:, (i % 2) * D:(i % 2 + 1) * D], h3[b][:, c, tile],
                                                    w3[a][:, c, :], start=(m == 0), stop=(m == 3 * FK - 1))
                            m += 1
                    if i % 2:
                        last.then_inc(y_ready, 1)

            chunks(pe, body)

        @block.scalar
        def _(act):
            for p, (name, k, _, _) in enumerate(pieces):
                if p >= 2:
                    act.wait_ge(weight_split, 2 * (p - 1))
                if name == "h2T":
                    act.dma_start(stage[:, p % 2, :], io[name][k * P:(k + 1) * P, :]).then_inc(staged[p % 2], 16)
                else:
                    act.dma_start(stage[:, p % 2, :].rearrange("p (c o) -> p c o", o=D),
                                  io[name][4 * k * P:4 * (k + 1) * P, :].rearrange("(c p) o -> p c o", p=P)
                                  ).then_inc(staged[p % 2], 16)
            act.sem_inc(hid_taken, 4)
            act.wait_ge(consts_loaded, 32)

            def body(n, u, prepare, fetch):
                for k in range(FK):
                    act.wait_ge(hid_ready, n * FK + (k + 1 + FK))
                    act.wait_ge(h3_ready, n * FK + (k + 1))
                    nc.scalar.activation(h3f[:, k % 2, :], hb[k % 4][:, :], ACT.Gelu, scale=hs[:, k:k + 1]
                                         ).then_inc(hid_taken, 1)

            chunks(act, body)

        @block.vector
        def _(dve):
            dve.sem_inc(h3_ready, 2)

            def split_h2(m, u):
                dve.wait_ge(h2_loaded[u], h2_count(m, u))
                dve.wait_ge(hid_ready, m * FK + FK)
                for k in range(FK):
                    nc.vector.tensor_copy(h2[0][:, k, :], h2f[:, u, k, :]).then_inc(h2_high, 1)
                    dve.wait_ge(h2_high, m * FK + (k + 1))
                    nc.vector.tensor_tensor(h2[1][:, k, :], h2f[:, u, k, :], h2[0][:, k, :].bitcast(F32),
                                            ALU.subtract).then_inc(h2_ready, 1)

            def body(n, u, prepare, fetch):
                dve.wait_ge(y_ready, n * 2 + 2)
                for k in range(FK):
                    dve.wait_ge(hid_taken, n * FK + (k + 1 + 4))
                    nc.vector.tensor_copy(h3[0][:, k, :], h3f[:, k % 2, :]).then_inc(h3_high, 1)
                    dve.wait_ge(h3_high, n * FK + (k + 1))
                    nc.vector.tensor_tensor(h3[1][:, k, :], h3f[:, k % 2, :], h3[0][:, k, :].bitcast(F32),
                                            ALU.subtract).then_inc(h3_ready, 1)
                if prepare:
                    split_h2(n + 1, 1 - u)
                dve.wait_ge(x1_loaded, n * 16 + 16)
                dve.wait_ge(out_stored, n * 16 + 16)
                for i in range(TPC):
                    if i % 2 == 0:
                        dve.wait_ge(y_ready, n * 2 + (i // 2 + 1 + 2))
                    last = nc.vector.tensor_tensor(y[:, i, :], yb[i // 2][:, (i % 2) * D:(i % 2 + 1) * D], s3[:, :],
                                                   ALU.mult)
                last.then_inc(step, 1)
                dve.wait_ge(step, n * NORM + 1)
                nc.vector.tensor_tensor(y[:, :, :], y[:, :, :], x1[:, :, :], ALU.add).then_inc(y_scaled, 1)
                dve.wait_ge(y_scaled, n + 1)
                for i in range(TPC):
                    last = nc.vector.bn_stats(stats[:, i, :], y[:, i, :])
                last.then_inc(step, 1)
                dve.wait_ge(step, n * NORM + 2)
                dve.sem_inc(stats_passed, 1)
                for i in range(TPC):
                    last = nc.vector.bn_aggr(mv[:, i, :], stats[:, i, :])
                last.then_inc(step, 1)
                dve.wait_ge(step, n * NORM + 3)
                nc.vector.tensor_scalar(var[:, :], mv[:, :, 1], EPS, None, ALU.add).then_inc(var_ready, 1)
                dve.wait_ge(rstd_ready, n + 1)
                for i in range(TPC):
                    nc.vector.tensor_scalar(y[:, i, :], y[:, i, :], mv[:, i, 0:1], rstd[:, i:i + 1],
                                            ALU.subtract, ALU.mult).then_inc(out_ready, 1)

            dve.wait_ge(consts_loaded, 32)
            for p, (name, k, high, low) in enumerate(pieces):
                src = stage[:, p % 2, :]
                if name == "w3T":
                    src = src.rearrange("p (c o) -> p c o", o=D)
                dve.wait_ge(staged[p % 2], 16 * (p // 2 + 1))
                nc.vector.tensor_copy(high, src).then_inc(weight_split, 1)
                dve.wait_ge(weight_split, 2 * p + 1)
                nc.vector.tensor_tensor(low, src, high.bitcast(F32), ALU.subtract).then_inc(weight_split, 1)
                if p == FK - 1:
                    split_h2(0, 0)
            chunks(dve, body)


_SHAPES = {
    "x": [T, D], "xT": [NCH, P, DH, CH], "cos": [NCH, P, CH], "sin": [NCH, P, CH],
    "WqT": [D, D], "WkT": [D, D], "WvT": [D, D], "WoT": [D, D],
    "bias": [P, 4 * DH], "sign": [P, 1], "bv": [D], "bo": [D],
    "ident": [P, P], "mask": [P, P], "spread": [P, P],
    "w1T": [D, F], "w2T": [D, F], "h1T": [F, F], "h2T": [F, F], "w3T": [F, D],
    "s1": [P, FK], "s2": [P, FK], "hs1": [P, FK], "hs2": [P, FK], "s3": [D],
}


def build(nc, io, out):
    qp_d = nc.dram_tensor("q_parts", [PARTS, D, NCH, CH], BF16, kind="Internal").ap()
    kp_d = nc.dram_tensor("k_parts", [PARTS, D, NCH, CH], BF16, kind="Internal").ap()
    v_d = nc.dram_tensor("values", [NQUAD, P, NCH, TPC, QUAD * VW], F32, kind="Internal").ap()
    max_d = nc.dram_tensor("maxima", [NCH, PARTS, QUAD * CH], BF16, kind="Internal").ap()
    o_d = nc.dram_tensor("outputs", [NCH, NQUAD, P, CH], F32, kind="Internal").ap()
    x1_d = nc.dram_tensor("x1", [NCH, P, TPC, D], F32, kind="Internal").ap()
    h2_d = nc.dram_tensor("hidden2", [NCH, P, FK, CH], F32, kind="Internal").ap()
    project(nc, io, qp_d, kp_d, v_d)
    attend(nc, io, qp_d, kp_d, v_d, max_d, o_d)
    widen(nc, io, o_d, x1_d, h2_d)
    narrow(nc, io, x1_d, h2_d, out)


def shape_constants():
    theta = np.float32(2500.0) ** (np.float32(-2.0) * np.arange(HD // 2, dtype=np.float32) / np.float32(HD))
    angle = np.arange(1, T + 1, dtype=np.float32)[None, :] * np.tile(theta, P // (HD // 2))[:, None]
    tables = {k: f(angle).astype(np.float32).reshape(P, NCH, CH).transpose(1, 0, 2)
              for k, f in (("cos", np.cos), ("sin", np.sin))}
    p = np.arange(P)
    spread = ((p[:, None] % 32 == HD) & (p[:, None] // 32 == p[None, :] // 32)).astype(np.float32)
    return dict(
        tables,
        sign=np.where(p % HD < HD // 2, -1.0, 1.0).astype(np.float32)[:, None],
        ident=np.eye(P, dtype=np.float32),
        mask=np.where(p[:, None] > p[None, :], MASKED, 0.0).astype(np.float32),
        spread=spread,
    )


def kernel(**inputs):
    import concourse.bacc as bacc
    from concourse.bass_utils import run_bass_kernel_spmd

    a = {k: np.asarray(v) for k, v in inputs.items()}
    x = a["L0_attn_x"].reshape(T, D)

    def exchanged(b):
        return b.reshape(HEADS, 2, HD // 2)[:, ::-1].reshape(D)

    def columns(v):
        return v.reshape(-1, P).T

    arrays = dict(
        shape_constants(),
        x=x,
        xT=x.reshape(NCH, CH, DH, P).transpose(0, 3, 2, 1),
        bias=np.concatenate([columns(v) for b in ("L0_attn_bq", "L0_attn_bk") for v in (a[b], exchanged(a[b]))], axis=1),
        bv=a["L0_attn_bv"], bo=a["L0_attn_bo"],
        WqT=a["L0_attn_Wq"].T, WkT=a["L0_attn_Wk"].T, WvT=a["L0_attn_Wv"].T, WoT=a["L0_attn_Wo"].T,
        w1T=a["L0_ffn_w1_w"].T, w2T=a["L0_ffn_w2_w"].T, h1T=a["L0_ffn_h1_w"].T, h2T=a["L0_ffn_h2_w"].T,
        w3T=a["L0_ffn_w3_w"].T, s1=columns(a["L0_ffn_w1_s"]), s2=columns(a["L0_ffn_w2_s"]),
        hs1=columns(a["L0_ffn_h1_s"]), hs2=columns(a["L0_ffn_h2_s"]), s3=a["L0_ffn_w3_s"],
    )
    arrays = {"in_" + k: np.ascontiguousarray(v) for k, v in arrays.items()}
    nc = bacc.Bacc("TRN2", target_bir_lowering=False, num_devices=1)
    io = {k: nc.dram_tensor("in_" + k, s, F32, kind="ExternalInput").ap() for k, s in _SHAPES.items()}
    out = nc.dram_tensor("out", [T, D], F32, kind="ExternalOutput").ap()
    build(nc, io, out)
    result = run_bass_kernel_spmd(nc, [arrays], core_ids=[0])
    return result.results[0]["out"].reshape(1, T, D)
```
